# Optimizing a Trainium2 kernel written in Bass

```python
import numpy as np
import jax
import jax.numpy as jnp

def _softmax(x, axis=-1):
    return jax.nn.softmax(x, axis=axis)

def _gelu(x):
    return jax.nn.gelu(x, approximate=True)

def _silu(x):
    return jax.nn.silu(x)

def _sigmoid(x):
    return jax.nn.sigmoid(x)

def _layernorm(x, axis=-1, eps=1e-05):
    m = jnp.mean(x, axis=axis, keepdims=True)
    v = jnp.var(x, axis=axis, keepdims=True)
    return (x - m) / jnp.sqrt(v + eps)

def _scatter_add(tgt, idx, src, axis=0):
    return tgt.at[idx].add(src)

def _segment_sum(src, seg, n):
    return jax.ops.segment_sum(src, seg, n)
kernel_name = 'mk_cond_resid_d2_seqx_r8_648957'

def setup_inputs(seed: int=0):
    np.random.seed(seed)
    _w = jnp.asarray

    def _rec_inputs():
        import jax
        import jax.numpy as jnp
        _rk = jax.random.key(seed)
        x = -7.109e-05 + 0.9999 * jax.random.normal(jax.random.fold_in(_rk, 1), (64, 32, 512), jnp.float32)
        _lenS = 32 - jax.random.randint(jax.random.fold_in(_rk, 7), (64,), 0, max(1, 32 // 4) + 1, jnp.int32)
        _lenS2 = 32 - jax.random.randint(jax.random.fold_in(_rk, 8), (64,), 0, max(1, 32 // 4) + 1, jnp.int32)
        itok_B_0_15 = jax.random.randint(jax.random.fold_in(_rk, 11), (64,), 0, 16, jnp.int32)
        itok_B_0_23 = jax.random.randint(jax.random.fold_in(_rk, 12), (64,), 0, 24, jnp.int32)
        return (x, itok_B_0_15, itok_B_0_23)
    x, itok_B_0_15, itok_B_0_23 = _rec_inputs()

    def _L0_cond_setup():
        import jax, jax.numpy as jnp
        import numpy as np
        B, C, T = (64, 32, 512)
        S, D = (16, 32)
        key = jax.random.key(seed)
        k1, k2, k3 = jax.random.split(key, 3)
        x = jax.random.normal(k1, (B, C, T), dtype=jnp.float32)
        condition = jax.random.randint(k2, (B,), 0, S, dtype=jnp.int64)
        bound = float(np.sqrt(6.0 / C))
        weights = jax.random.uniform(k3, (S, C, D), dtype=jnp.float32, minval=-bound, maxval=bound)
        return {'x': x, 'condition': condition, 'weights': weights}
    _L0_cond_all = _L0_cond_setup()
    _L0_cond_in = {k: v for k, v in _L0_cond_all.items() if k in ('weights',)}
    del _L0_cond_all

    def _L1_cond_setup():
        import jax, jax.numpy as jnp
        import numpy as np
        R = 16
        ALPHA = 32
        SCALING = ALPHA / R
        SLOTS = 32
        IN_F = 512
        OUT_F = 512
        B, T = (8, 128)
        key = jax.random.key(seed)
        k1, k2, k3, k4, k5, k6 = jax.random.split(key, 6)
        x = jax.random.normal(k1, (B, T, IN_F), dtype=jnp.float32)
        adapter_mapping = jax.random.randint(k2, (B,), 0, SLOTS, dtype=jnp.int32)
        W = jax.random.normal(k3, (OUT_F, IN_F), dtype=jnp.float32) * 0.02
        b = jax.random.normal(k4, (OUT_F,), dtype=jnp.float32) * 0.02
        lora_As = jax.random.normal(k5, (SLOTS, IN_F, R), dtype=jnp.float32) * 0.02
        lora_Bs = jax.random.normal(k6, (SLOTS, R, OUT_F), dtype=jnp.float32) * 0.02
        return {'x': x, 'adapter_mapping': adapter_mapping, 'W': W, 'b': b, 'lora_As': lora_As, 'lora_Bs': lora_Bs}
    _L1_cond_all = _L1_cond_setup()
    _L1_cond_in = {k: v for k, v in _L1_cond_all.items() if k in ('W', 'b', 'lora_As', 'lora_Bs')}
    del _L1_cond_all
    return {'x': x, 'itok_B_0_15': itok_B_0_15, 'itok_B_0_23': itok_B_0_23, 'L0_cond_weights': _L0_cond_in['weights'], 'L1_cond_W': _L1_cond_in['W'], 'L1_cond_b': _L1_cond_in['b'], 'L1_cond_lora_As': _L1_cond_in['lora_As'], 'L1_cond_lora_Bs': _L1_cond_in['lora_Bs']}

def reference(x, itok_B_0_15, itok_B_0_23, L0_cond_weights, L1_cond_W, L1_cond_b, L1_cond_lora_As, L1_cond_lora_Bs):
    import jax
    import jax.numpy as jnp

    def _L0_cond_ref(x, condition, weights):
        import jax, jax.numpy as jnp
        import numpy as np
        B, C, T = (64, 32, 512)
        S, D = (16, 32)
        W = weights[condition]
        return jnp.einsum('bct,bcd->bdt', x, W)

    def _L1_cond_ref(x, adapter_mapping, W, b, lora_As, lora_Bs):
        import jax, jax.numpy as jnp
        import numpy as np
        R = 16
        ALPHA = 32
        SCALING = ALPHA / R
        SLOTS = 32
        IN_F = 512
        OUT_F = 512
        B, T = (8, 128)
        base_out = jnp.einsum('bti,oi->bto', x, W) + b
        A = lora_As[adapter_mapping]
        Bm = lora_Bs[adapter_mapping]
        lora_h = jnp.einsum('bti,bir->btr', x, A)
        lora_out = jnp.einsum('btr,bro->bto', lora_h, Bm)
        return base_out + lora_out * SCALING
    x = x + _L0_cond_ref(x, itok_B_0_15, L0_cond_weights)
    x = x + _L1_cond_ref(x, itok_B_0_23, L1_cond_W, L1_cond_b, L1_cond_lora_As, L1_cond_lora_Bs)
    return x

_drawn_inputs = setup_inputs


def setup_inputs(seed=0):
    import zlib

    import numpy as np

    out = dict(_drawn_inputs(seed))
    spreads = {}
    factors = {'L1_cond_b': 5.712}
    for name, (base, spread) in spreads.items():
        noise = np.random.default_rng([zlib.crc32(name.encode()), seed]).standard_normal(out[name].shape)
        drawn = base * np.exp(spread * noise) if base else spread * noise
        out[name] = jnp.asarray(drawn.astype(out[name].dtype))
    for name, factor in factors.items():
        out[name] = (out[name] * factor).astype(out[name].dtype)
    return out
```

```python
from contextlib import ExitStack

import concourse.bass as bass
from concourse import mybir

F32 = mybir.dt.float32
F32R = mybir.dt.float32r
I32 = mybir.dt.int32
U32 = mybir.dt.uint32
ALU = mybir.AluOpType
AX_X = mybir.AxisListType.X

P = 128
ALPHA = 32


def lora_residual_program(nc, x, cond, adapter, w0, w, bias, lora_a, lora_b, out):
    B, C, T = x.shape
    S0 = w0.shape[0]
    SLOTS, _, R = lora_a.shape
    O = w.shape[0]
    SCALING = float(ALPHA // R)
    J = P // C
    TILES = B // J
    KC = T // P
    HALF = O // 2
    HJ = J // 2
    AC = HJ * R
    NW = AC + HALF
    WROW = AC + HALF + AC
    A_AT = (0, AC + HALF)
    MOV = (0, AC)
    H_PS = (0, HALF)
    Y_PS = (AC, 0)
    assert C == 32 and 2 * R == 32 and J == 4 and O == T == 512 and TILES % 2 == 0

    x_rows = x.rearrange("b c t -> (b c) t")
    out_rows = out.rearrange("b c t -> (b c) t")

    with ExitStack() as ctx:
        def sb(name, shape, dt):
            return ctx.enter_context(nc.sbuf_tensor(name, shape, dt))

        def sem(name):
            return ctx.enter_context(nc.semaphore(name))

        ident = sb("ident", [P, P], F32)
        own_mask = sb("own_mask", [P, P], F32)
        pick = sb("pick", [P, J], F32)
        part = sb("part", [P, 1], I32)
        r_int = sb("r_int", [P, 1], I32)
        r_of_p = sb("r_of_p", [P, 1], F32)
        eye32 = sb("eye32", [P, C], F32)
        cond_sb = sb("cond_sb", [1, B], I32)
        ad_sb = sb("ad_sb", [P, B], I32)
        ad_pick = sb("ad_pick", [P, TILES, J], F32)
        ad_row = sb("ad_row", [P, TILES], F32)
        b_index = sb("b_index", [P, TILES], U32)
        b_index_slot = [sb(f"b_index_slot{s}", [P, 1], U32) for s in range(2)]
        w0_all = sb("w0_all", [P, S0, C], F32)
        m_blocks = [sb(f"m_blocks{s}", [P, P], F32) for s in range(2)]
        w_nat = sb("w_nat", [P, KC, T], F32)
        wa = sb("wa", [P, KC, 2, 2, WROW], F32R)
        a_raw = sb("a_raw", [P, SLOTS * KC, R], F32)
        a_split = sb("a_split", [P, SLOTS * KC, 2, R], F32R)
        bias_sb = sb("bias_sb", [P, O], F32)
        b_raw = [sb(f"b_raw{s}", [P, O], F32) for s in range(2)]
        b_hi = [sb(f"b_hi{s}", [P, O], F32R) for s in range(2)]
        b_lo = [sb(f"b_lo{s}", [P, O], F32R) for s in range(2)]
        x_sb = [sb(f"x_sb{s}", [P, T], F32) for s in range(2)]
        x1_hi = [sb(f"x1_hi{s}", [P, T], F32R) for s in range(2)]
        x1_lo = [sb(f"x1_lo{s}", [P, T], F32R) for s in range(2)]
        h_split = [sb(f"h_split{s}", [P, J, 2, R], F32) for s in range(2)]
        ht_sb = [sb(f"ht_sb{s}", [P, P], F32R) for s in range(2)]
        y_sb = [sb(f"y_sb{s}", [P, O], F32) for s in range(2)]

        y_ps = [ctx.enter_context(nc.psum_tensor(f"y_ps{s}", [P, 2, 512], F32)) for s in range(2)]
        x1_ps = [ctx.enter_context(nc.psum_tensor(f"x1_ps{s}", [P, T], F32)) for s in range(2)]
        ht_ps = [ctx.enter_context(nc.psum_tensor(f"ht_ps{s}", [P, 512], F32)) for s in range(2)]

        cond_loaded = sem("cond_loaded")
        ad_loaded = sem("ad_loaded")
        w0_loaded = sem("w0_loaded")
        w_loaded = [sem(f"w_loaded{c}") for c in range(KC)]
        a_loaded = sem("a_loaded")
        bias_loaded = sem("bias_loaded")
        x_loaded = [sem(f"x_loaded{s}") for s in range(2)]
        b_gathered = [sem(f"b_gathered{s}") for s in range(2)]
        y_stored = [sem(f"y_stored{s}") for s in range(2)]
        ident_zero = sem("ident_zero")
        ident_ready = sem("ident_ready")
        part_ready = sem("part_ready")
        m_zero = sem("m_zero")
        dve_chain = sem("dve_chain")
        w0_ready = sem("w0_ready")
        w_plus_i = sem("w_plus_i")
        wt_ps_ready = sem("wt_ps_ready")
        w_hi_ready = sem("w_hi_ready")
        w_ready = sem("w_ready")
        a_hi_ready = sem("a_hi_ready")
        a_split_ready = sem("a_split_ready")
        b_index_ready = sem("b_index_ready")
        b_index_copied = sem("b_index_copied")
        m_ready = sem("m_ready")
        a_ready = sem("a_ready")
        b_hi_ready = sem("b_hi_ready")
        b_ready = sem("b_ready")
        x1_computed = sem("x1_computed")
        x1_hi_ready = sem("x1_hi_ready")
        x1_ready = sem("x1_ready")
        main_done = sem("main_done")
        h_hi_ready = sem("h_hi_ready")
        h_ready = sem("h_ready")
        ht_computed = sem("ht_computed")
        ht_ready = sem("ht_ready")
        lora_done = sem("lora_done")
        y_ready = sem("y_ready")


        block = ctx.enter_context(nc.Block())

        @block.sync
        def _(sp):
            sp.dma_start(cond_sb[:, :], cond.rearrange("(a b) -> a b", a=1)).then_inc(cond_loaded, 16)
            for j in range(J):
                sp.dma_start(w0_all[j * C:(j + 1) * C, :, :], w0.rearrange("s c d -> c s d")).then_inc(w0_loaded, 16)

            def load_x(u, s):
                sp.dma_start(x_sb[s][:, :], x_rows[bass.ds(u * P, P), :]).then_inc(x_loaded[s], 16)

            def store_y(u, s):
                sp.wait_ge(y_ready, u + 1)
                sp.dma_start(out_rows[bass.ds(u * P, P), :], y_sb[s][:, :]).then_inc(y_stored[s], 16)

            load_x(0, 0)
            load_x(1, 1)
            sp.dma_start(a_raw[:, :, :], lora_a.rearrange("s (k p) r -> p (s k) r", p=P)).then_inc(a_loaded, 16)
            sp.dma_start(bias_sb[:, :], bias.rearrange("(a o) -> a o", a=1).broadcast_to([P, O])).then_inc(bias_loaded, 16)
            sp.wait_ge(x1_computed, 1)
            load_x(2, 0)
            sp.wait_ge(x1_computed, 2)
            load_x(3, 1)
            with sp.Fori(0, TILES // 2 - 2) as i:
                for s in range(2):
                    u = 2 * i + s
                    store_y(u, s)
                    sp.wait_ge(x1_computed, u + 3)
                    load_x(u + 4, s)
            for u in range(TILES - 4, TILES):
                store_y(u, u % 2)
            for s in range(2):
                sp.wait_ge(y_stored[s], 16 * (TILES // 2))

        @block.gpsimd
        def _(pool):
            pool.memset(ident[:, :], 0.0).then_inc(ident_zero, 1)
            pool.wait_ge(ident_zero, 1)
            pool.affine_select(out=ident[:, :], in_=ident[:, :], compare_op=ALU.not_equal, fill=1.0,
                               base=0, pattern=[[-1, P]], channel_multiplier=1).then_inc(ident_ready, 1)
            pool.iota(part[:, :], pattern=[[0, 1]], base=0, channel_multiplier=1).then_inc(part_ready, 1)

            adapters = [pool.alloc_register(f"adapter{j}") for j in range(J)]

            def take_index(u, s, first=False):
                if not first:
                    pool.wait_ge(b_ready, u - 1)
                pool.tensor_copy(b_index_slot[s][:, :], b_index[:, bass.ds(u, 1)]).then_inc(b_index_copied, 1)

            def place_a(u, s, first=False):
                pool.load(adapters, ad_sb[0:1, bass.ds(u * J, J)])
                if not first:
                    pool.wait_ge(main_done, u - 1)
                    pool.wait_ge(b_index_copied, u + 1)
                for j in range(J):
                    slot = pool.snap(adapters[j], min_val=0, max_val=SLOTS - 1)
                    at = A_AT[s] + (j % HJ) * R
                    last = pool.tensor_copy(
                        wa[:, :, :, j // HJ, at:at + R],
                        a_split[:, bass.ds(slot * KC, KC), :, :])
                last.then_inc(a_ready, 1)

            def gather_b(s):
                pool.indirect_dma_start(
                    b_raw[s][:, :], None, lora_b.rearrange("s r o -> (s r) o"),
                    bass.IndirectOffsetOnAxis(ap=b_index_slot[s][:, 0:1], axis=0)).then_inc(b_gathered[s], 16)

            pool.wait_ge(b_index_ready, 1)
            take_index(0, 0, first=True)
            take_index(1, 1, first=True)
            pool.wait_ge(b_index_copied, 2)
            gather_b(0)
            gather_b(1)
            pool.wait_ge(a_split_ready, 1)
            place_a(0, 0, first=True)
            place_a(1, 1, first=True)
            with pool.Fori(1, TILES // 2) as i:
                for s in range(2):
                    u = 2 * i + s
                    take_index(u, s)
                    place_a(u, s)
                    gather_b(s)

        @block.scalar
        def _(act):
            act.dma_start(ad_sb[:, :], adapter.rearrange("(a b) -> a b", a=1).broadcast_to([P, B])).then_inc(ad_loaded, 16)
            for k in range(KC):
                act.dma_start(w_nat[:, k, :], w[k * P:(k + 1) * P, :]).then_inc(w_loaded[k], 16)

            conds = [act.alloc_register(f"cond{j}") for j in range(J)]

            def build_m(u, s, first=False):
                act.load(conds, cond_sb[0:1, bass.ds(u * J, J)])
                if not first:
                    act.wait_ge(x1_computed, u - 1)
                for j in range(J):
                    slot = act.snap(conds[j], min_val=0, max_val=S0 - 1)
                    q = slice(j * C, (j + 1) * C)
                    last = act.copy(m_blocks[s][q, j * C:(j + 1) * C], w0_all[q, bass.ds(slot, 1), :])
                last.then_inc(m_ready, 1)

            def round_x1(u, s, first=False):
                act.wait_ge(x1_computed, u + 1)
                if not first:
                    act.wait_ge(main_done, u - 1)
                act.copy(x1_hi[s][:, :], x1_ps[s][:, :]).then_inc(x1_hi_ready, 1)

            def round_b(u, s, n, first=False):
                act.wait_ge(b_gathered[s], 16 * (n + 1))
                if not first:
                    act.wait_ge(lora_done, u - 1)
                act.copy(b_hi[s][:, :], b_raw[s][:, :]).then_inc(b_hi_ready, 1)

            def round_h(u, s, first=False):
                act.wait_ge(main_done, u + 1)
                if not first:
                    act.wait_ge(ht_computed, u - 1)
                act.copy(h_split[s][:, :, 0, :].rearrange("p (a j) r -> p a j r", a=2),
                         y_ps[s][:, :, H_PS[s]:H_PS[s] + AC].rearrange("p a (j r) -> p a j r", j=HJ)
                         ).then_inc(h_hi_ready, 1)

            act.wait_ge(cond_loaded, 16)
            act.wait_ge(w0_ready, 1)
            act.wait_ge(m_zero, 2)
            build_m(0, 0, first=True)
            build_m(1, 1, first=True)
            for k in range(KC):
                act.wait_ge(wt_ps_ready, k + 1)
                act.copy(wa[:, k, 0, :, AC:AC + HALF],
                         y_ps[k // 2][:, k % 2, :].rearrange("p (a o) -> p a o", a=2)).then_inc(w_hi_ready, 1)
            round_x1(0, 0, first=True)
            act.wait_ge(a_loaded, 16)
            act.copy(a_split[:, :, 0, :], a_raw[:, :, :]).then_inc(a_hi_ready, 1)
            round_x1(1, 1, first=True)
            build_m(2, 0)
            round_b(0, 0, 0, first=True)
            def step(u, s, n, first=False, more_x=True, more_m=True):
                round_h(u - 1, 1 - s, first=first)
                if more_x:
                    round_x1(u + 1, 1 - s)
                if more_m:
                    build_m(u + 2, s)
                round_b(u, s, n, first=first)

            step(1, 1, 0, first=True)
            step(2, 0, 1, first=True)
            with act.Fori(1, TILES // 2 - 2) as i:
                step(2 * i + 1, 1, i)
                step(2 * i + 2, 0, i + 1)
            step(TILES - 3, 1, TILES // 2 - 2)
            step(TILES - 2, 0, TILES // 2 - 1, more_m=False)
            step(TILES - 1, 1, TILES // 2 - 1, more_x=False, more_m=False)
            round_h(TILES - 1, 1)

        @block.vector
        def _(dve):
            chained = [0]

            def link(ins):
                chained[0] += 1
                ins.then_inc(dve_chain, 1)
                dve.wait_ge(dve_chain, chained[0])

            for s in range(2):
                nc.vector.memset(m_blocks[s][:, :], 0.0).then_inc(m_zero, 1)
            nc.vector.memset(pick[:, :], 0.0)
            link(nc.vector.memset(own_mask[:, :], 0.0))
            for j in range(J):
                q = slice(j * C, (j + 1) * C)
                nc.vector.memset(own_mask[q, q], SCALING)
                last = nc.vector.memset(pick[q, j:j + 1], float(R))
            link(last)
            dve.wait_ge(part_ready, 1)
            link(nc.vector.tensor_single_scalar(r_int[:, :], part[:, :], R - 1, ALU.bitwise_and))
            link(nc.vector.tensor_copy(r_of_p[:, :], r_int[:, :]))
            dve.wait_ge(ad_loaded, 16)
            link(nc.vector.tensor_tensor(ad_pick[:, :, :], ad_sb[:, :].rearrange("p (u j) -> p u j", j=J),
                                         pick[:, :].rearrange("p (a j) -> p a j", a=1).broadcast_to([P, TILES, J]), ALU.mult))
            link(nc.vector.reduce_sum(ad_row[:, :], ad_pick[:, :, :], AX_X))
            nc.vector.tensor_scalar(b_index[:, :], ad_row[:, :], r_of_p[:, 0:1], None,
                                    ALU.add).then_inc(b_index_ready, 1)
            dve.wait_ge(ident_ready, 1)
            for j in range(J):
                q = slice(j * C, (j + 1) * C)
                last = nc.vector.tensor_copy(eye32[q, :], ident[q, q])
            link(last)
            dve.wait_ge(w0_loaded, 16 * J)
            nc.vector.tensor_tensor(w0_all[:, :, :], w0_all[:, :, :],
                                    eye32[:, :].rearrange("p (a d) -> p a d", a=1).broadcast_to([P, S0, C]),
                                    ALU.add).then_inc(w0_ready, 1)
            for k in range(KC):
                dve.wait_ge(w_loaded[k], 16)
                nc.vector.tensor_tensor(w_nat[:, k, k * P:(k + 1) * P], w_nat[:, k, k * P:(k + 1) * P],
                                        ident[:, :], ALU.add).then_inc(w_plus_i, 1)
            for k in range(KC):
                dve.wait_ge(w_hi_ready, k + 1)
                nc.vector.tensor_tensor(wa[:, k, 1, :, AC:AC + HALF],
                                        y_ps[k // 2][:, k % 2, :].rearrange("p (a o) -> p a o", a=2),
                                        wa[:, k, 0, :, AC:AC + HALF], ALU.subtract).then_inc(w_ready, 1)

            def rest_x1(u, s):
                dve.wait_ge(x1_hi_ready, u + 1)
                nc.vector.tensor_tensor(x1_lo[s][:, :], x1_ps[s][:, :], x1_hi[s][:, :],
                                        ALU.subtract).then_inc(x1_ready, 1)

            def rest_b(u, s):
                dve.wait_ge(b_hi_ready, u + 1)
                nc.vector.tensor_tensor(b_lo[s][:, :], b_raw[s][:, :], b_hi[s][:, :],
                                        ALU.subtract).then_inc(b_ready, 1)

            def rest_h(u, s):
                dve.wait_ge(h_hi_ready, u + 1)
                nc.vector.tensor_tensor(
                    h_split[s][:, :, 1, :].rearrange("p (a j) r -> p a j r", a=2),
                    y_ps[s][:, :, H_PS[s]:H_PS[s] + AC].rearrange("p a (j r) -> p a j r", j=HJ),
                    h_split[s][:, :, 0, :].rearrange("p (a j) r -> p a j r", a=2),
                    ALU.subtract).then_inc(h_ready, 1)

            def mask_ht(u, s, first=False):
                dve.wait_ge(ht_computed, u + 1)
                if not first:
                    dve.wait_ge(lora_done, u - 1)
                nc.vector.tensor_tensor(ht_sb[s][:, :], ht_ps[s][:, 0:P], own_mask[:, :],
                                        ALU.mult).then_inc(ht_ready, 1)

            def finish_y(u, s, n, first=False):
                dve.wait_ge(lora_done, u + 1)
                if not first:
                    dve.wait_ge(y_stored[s], 16 * n)
                nc.vector.tensor_tensor(
                    y_sb[s][:, :].rearrange("p (a o) -> p a o", a=2),
                    y_ps[s][:, :, Y_PS[s]:Y_PS[s] + HALF],
                    bias_sb[:, :].rearrange("p (a o) -> p a o", a=2), ALU.add).then_inc(y_ready, 1)

            rest_x1(0, 0)
            dve.wait_ge(a_hi_ready, 1)
            nc.vector.tensor_tensor(a_split[:, :, 1, :], a_raw[:, :, :], a_split[:, :, 0, :],
                                    ALU.subtract).then_inc(a_split_ready, 1)
            rest_x1(1, 1)
            rest_b(0, 0)
            dve.wait_ge(bias_loaded, 16)

            def step(u, s, n, first=False, more_x=True):
                rest_h(u - 1, 1 - s)
                mask_ht(u - 1, 1 - s, first=first)
                if more_x:
                    rest_x1(u + 1, 1 - s)
                rest_b(u, s)
                finish_y(u - 1, 1 - s, n, first=first)

            step(1, 1, 0, first=True)
            step(2, 0, 0, first=True)
            with dve.Fori(1, TILES // 2 - 1) as i:
                step(2 * i + 1, 1, i)
                step(2 * i + 2, 0, i)
            step(TILES - 1, 1, TILES // 2 - 1, more_x=False)
            rest_h(TILES - 1, 1)
            mask_ht(TILES - 1, 1)
            finish_y(TILES - 1, 1, TILES // 2 - 1)

        @block.tensor
        def _(pe):
            def x1_of(u, s, n, first=False):
                pe.wait_ge(x_loaded[s], 16 * (n + 1))
                pe.wait_ge(m_ready, u + 1)
                if not first:
                    pe.wait_ge(x1_ready, u - 1)
                for k in range(KC):
                    last = nc.tensor.matmul(x1_ps[s][:, k * P:(k + 1) * P], x_sb[s][:, k * P:(k + 1) * P],
                                            m_blocks[s][:, :], start=True, stop=True)
                last.then_inc(x1_computed, 1)

            def main_chunk(s, k):
                for half in range(2):
                    for lo_x, lo_w in ((0, 0), (0, 1), (1, 0)):
                        last = nc.tensor.matmul(
                            y_ps[s][:, half, 0:NW], (x1_lo if lo_x else x1_hi)[s][:, k * P:(k + 1) * P],
                            wa[:, k, lo_w, half, MOV[s]:MOV[s] + NW],
                            start=(k == 0 and not lo_x and not lo_w), stop=(k == KC - 1 and lo_x == 1),
                            skip_group_check=True)
                return last

            def main_first(u, s, first=False):
                pe.wait_ge(x1_ready, u + 1)
                pe.wait_ge(a_ready, u + 1)
                if not first:
                    pe.wait_ge(y_ready, u - 1)
                main_chunk(s, 0)

            def transpose_h(u, s):
                pe.wait_ge(h_ready, u + 1)
                nc.tensor.transpose(ht_ps[s][:, 0:P], h_split[s][:, :, :, :].rearrange("p j e r -> p (j e r)"),
                                    ident[:, :]).then_inc(ht_computed, 1)

            def lora(u, s):
                pe.wait_ge(ht_ready, u + 1)
                pe.wait_ge(b_ready, u + 1)
                for half in range(2):
                    for b_part in (b_hi, b_lo):
                        last = nc.tensor.matmul(
                            y_ps[s][:, half, Y_PS[s]:Y_PS[s] + HALF], ht_sb[s][:, :],
                            b_part[s][:, half * HALF:(half + 1) * HALF], start=False, stop=True,
                            skip_group_check=True)
                last.then_inc(lora_done, 1)

            pe.wait_ge(w_plus_i, KC)
            for k in range(KC):
                for ok in range(KC):
                    last = nc.tensor.transpose(y_ps[k // 2][:, k % 2, ok * P:(ok + 1) * P],
                                               w_nat[:, ok, k * P:(k + 1) * P], ident[:, :])
                last.then_inc(wt_ps_ready, 1)
            x1_of(0, 0, 0, first=True)
            x1_of(1, 1, 0, first=True)
            pe.wait_ge(w_ready, KC)
            main_first(0, 0, first=True)
            for k in range(1, KC):
                last = main_chunk(0, k)
            last.then_inc(main_done, 1)
            x1_of(2, 0, 1)

            def step(u, s, n_x=None, first=False):
                main_first(u, s, first=first)
                transpose_h(u - 1, 1 - s)
                main_chunk(s, 1)
                main_chunk(s, 2)
                lora(u - 1, 1 - s)
                main_chunk(s, 3).then_inc(main_done, 1)
                if n_x is not None:
                    x1_of(u + 2, s, n_x)

            step(1, 1, 1, first=True)
            step(2, 0, 2)
            with pe.Fori(1, TILES // 2 - 2) as i:
                step(2 * i + 1, 1, i + 1)
                step(2 * i + 2, 0, i + 2)
            step(TILES - 3, 1, TILES // 2 - 1)
            step(TILES - 2, 0)
            step(TILES - 1, 1)
            transpose_h(TILES - 1, 1)
            lora(TILES - 1, 1)


_INS = ["x", "itok_B_0_15", "itok_B_0_23", "L0_cond_weights", "L1_cond_W", "L1_cond_b",
        "L1_cond_lora_As", "L1_cond_lora_Bs"]


def kernel(**inputs):
    import numpy as _np
    import concourse.bacc as _bacc
    from concourse import mybir as _mybir
    from concourse.bass_utils import run_bass_kernel_spmd as _run

    nc = _bacc.Bacc("TRN2", target_bir_lowering=False, num_devices=1)
    arrays, args = {}, []
    for name in _INS:
        a = _np.ascontiguousarray(inputs[name])
        arrays[f"in_{name}"] = a
        args.append(nc.dram_tensor(f"in_{name}", a.shape, _mybir.dt.from_np(a.dtype), kind="ExternalInput").ap())
    shape = inputs["x"].shape
    args.append(nc.dram_tensor("out", shape, _mybir.dt.float32, kind="ExternalOutput").ap())
    lora_residual_program(nc, *args)
    r = _run(nc, [arrays], core_ids=[0])
    return r.results[0]["out"]
```

```python
from contextlib import ExitStack

import concourse.bass as bass
from concourse import mybir

F32 = mybir.dt.float32
F32R = mybir.dt.float32r
BF16 = mybir.dt.bfloat16
I32 = mybir.dt.int32
U32 = mybir.dt.uint32
ALU = mybir.AluOpType
AX_X = mybir.AxisListType.X

P = 128
ALPHA = 32


def lora_residual_program(nc, x, cond, adapter, w0, w, bias, lora_a, lora_b, out):
    B, C, T = x.shape
    S0 = w0.shape[0]
    SLOTS, _, R = lora_a.shape
    O = w.shape[0]
    SCALING = float(ALPHA // R)
    J = P // C
    TILES = B // J
    KC = T // P
    KM = KC // 2
    TM = T // KM
    A_GROUPS = 4
    WARM_UP = 14
    HALF = O // 2
    HJ = J // 2
    AC = HJ * R
    NW = AC + HALF
    WROW = AC + HALF + AC
    A_AT = (0, AC + HALF)
    MOV = (0, AC)
    H_PS = (0, HALF)
    Y_PS = (AC, 0)
    assert C == 32 and 2 * R == 32 and J == 4 and O == T == 512 and TILES % 2 == 0

    x_rows = x.rearrange("b c t -> (b c) t")
    out_rows = out.rearrange("b c t -> (b c) t")

    with ExitStack() as ctx:
        def sb(name, shape, dt):
            return ctx.enter_context(nc.sbuf_tensor(name, shape, dt))

        def sem(name):
            return ctx.enter_context(nc.semaphore(name))

        ident = sb("ident", [P, P], F32)
        own_mask = sb("own_mask", [P, P], F32)
        pick = sb("pick", [P, J], F32)
        part = sb("part", [P, 1], I32)
        r_int = sb("r_int", [P, 1], I32)
        r_of_p = sb("r_of_p", [P, 1], F32)
        zeros = sb("zeros", [P, 512], BF16)
        cond_sb = sb("cond_sb", [1, B], I32)
        ad_sb = sb("ad_sb", [P, B], I32)
        ad_pick = sb("ad_pick", [P, TILES, J], F32)
        ad_row = sb("ad_row", [P, TILES], F32)
        b_index = sb("b_index", [P, TILES], U32)
        b_index_slot = [sb(f"b_index_slot{s}", [P, 1], U32) for s in range(2)]
        w0_all = sb("w0_all", [C, S0, C], F32)
        m_blocks = [sb(f"m_blocks{s}", [P, P], F32) for s in range(2)]
        w_nat = sb("w_nat", [P, KC, T], F32)
        wa = sb("wa", [P, KC, 2, 2, WROW], F32R)
        a_raw = sb("a_raw", [P, SLOTS * KC, R], F32)
        a_split = sb("a_split", [P, SLOTS * KC, 2, R], F32R)
        bias_sb = sb("bias_sb", [P, O], F32)
        b_raw = [sb(f"b_raw{s}", [P, O], F32) for s in range(2)]
        b_hi = [sb(f"b_hi{s}", [P, O], F32R) for s in range(2)]
        b_lo = [sb(f"b_lo{s}", [P, O], F32R) for s in range(2)]
        x_sb = [sb(f"x_sb{s}", [P, T], F32) for s in range(2)]
        x1_hi = [sb(f"x1_hi{s}", [P, T], F32R) for s in range(2)]
        x1_lo = [sb(f"x1_lo{s}", [P, T], F32R) for s in range(2)]
        h_split = [sb(f"h_split{s}", [P, J, 2, R], F32R) for s in range(2)]
        ht_sb = [sb(f"ht_sb{s}", [P, P], F32R) for s in range(2)]
        y_sb = [sb(f"y_sb{s}", [P, O], F32) for s in range(2)]

        y_ps = [ctx.enter_context(nc.psum_tensor(f"y_ps{s}", [P, 2, 512], F32)) for s in range(2)]
        x1_ps = [ctx.enter_context(nc.psum_tensor(f"x1_ps{s}", [P, T], F32)) for s in range(2)]
        ht_ps = [ctx.enter_context(nc.psum_tensor(f"ht_ps{s}", [P, 512], F32)) for s in range(2)]

        cond_loaded = sem("cond_loaded")
        ad_loaded = sem("ad_loaded")
        w0_loaded = sem("w0_loaded")
        w_loaded = [sem(f"w_loaded{m}") for m in range(KM)]
        a_loaded = [sem(f"a_loaded{g}") for g in range(A_GROUPS)]
        bias_loaded = sem("bias_loaded")
        x_loaded = [sem(f"x_loaded{s}") for s in range(2)]
        b_gathered = [sem(f"b_gathered{s}") for s in range(2)]
        y_stored = [sem(f"y_stored{s}") for s in range(2)]
        ident_zero = sem("ident_zero")
        ident_ready = sem("ident_ready")
        part_ready = sem("part_ready")
        zeros_ready = sem("zeros_ready")
        m_zero = sem("m_zero")
        dve_chain = sem("dve_chain")
        w0_ready = sem("w0_ready")
        w_plus_i = sem("w_plus_i")
        wt_ps_ready = sem("wt_ps_ready")
        w_hi_ready = sem("w_hi_ready")
        w_ready = sem("w_ready")
        a_hi_ready = sem("a_hi_ready")
        a_split_ready = sem("a_split_ready")
        b_index_ready = sem("b_index_ready")
        b_index_copied = sem("b_index_copied")
        m_ready = sem("m_ready")
        a0_ready = sem("a0_ready")
        a_ready = sem("a_ready")
        b_hi_ready = sem("b_hi_ready")
        b_ready = sem("b_ready")
        x1_computed = sem("x1_computed")
        x1_hi_ready = sem("x1_hi_ready")
        x1_ready = sem("x1_ready")
        main_done = sem("main_done")
        h_hi_ready = sem("h_hi_ready")
        h_ready = sem("h_ready")
        ht_computed = sem("ht_computed")
        ht_ready = sem("ht_ready")
        lora_done = sem("lora_done")
        y_ready = sem("y_ready")


        block = ctx.enter_context(nc.Block())

        def a_group(g):
            n = SLOTS // A_GROUPS * KC
            return slice(g * n, (g + 1) * n)

        def a_columns(s, j):
            at = A_AT[s] + (j % HJ) * R
            return slice(at, at + R)

        def h_of(s, alone):
            h = ht_ps[s][:, P:P + 2 * AC].rearrange("p (a c) -> p a c", a=2) if alone else \
                y_ps[s][:, :, H_PS[s]:H_PS[s] + AC]
            return h.rearrange("p a (j r) -> p a j r", j=HJ)

        def chunk_of_t(k):
            m, e = divmod(k, 2)
            return slice(m * TM + e, (m + 1) * TM, 2)

        @block.sync
        def _(sp):
            sp.dma_start(cond_sb[:, :], cond.rearrange("(a b) -> a b", a=1)).then_inc(cond_loaded, 16)
            sp.dma_start(w0_all[:, :, :], w0.rearrange("s c d -> c s d")).then_inc(w0_loaded, 16)

            def load_x(u, s):
                sp.dma_start(x_sb[s][:, :], x_rows[bass.ds(u * P, P), :]).then_inc(x_loaded[s], 16)

            def store_y(u, s):
                sp.wait_ge(y_ready, u + 1)
                sp.dma_start(out_rows[bass.ds(u * P, P), :], y_sb[s][:, :]).then_inc(y_stored[s], 16)

            load_x(0, 0)
            sp.dma_start(ad_sb[:, :], adapter.rearrange("(a b) -> a b", a=1).broadcast_to([P, B])).then_inc(ad_loaded, 16)
            load_x(1, 1)
            for g in range(A_GROUPS):
                n = SLOTS // A_GROUPS
                sp.dma_start(a_raw[:, a_group(g), :].rearrange("p (a e) r -> p a (e r)", e=2),
                             lora_a[g * n:(g + 1) * n].rearrange("s (m p e) r -> p (s m) (e r)", p=P, e=2)
                             ).then_inc(a_loaded[g], 16)
            sp.dma_start(bias_sb[:, :], bias.rearrange("(a o) -> a o", a=1).broadcast_to([P, O])).then_inc(bias_loaded, 16)
            sp.wait_ge(x1_computed, 1)
            load_x(2, 0)
            sp.wait_ge(x1_computed, 2)
            load_x(3, 1)
            with sp.Fori(0, TILES // 2 - 2) as i:
                for s in range(2):
                    u = 2 * i + s
                    store_y(u, s)
                    sp.wait_ge(x1_computed, u + 3)
                    load_x(u + 4, s)
            for u in range(TILES - 4, TILES):
                store_y(u, u % 2)
            for s in range(2):
                sp.wait_ge(y_stored[s], 16 * (TILES // 2))

        @block.gpsimd
        def _(pool):
            pool.memset(ident[:, :], 0.0).then_inc(ident_zero, 1)
            pool.wait_ge(ident_zero, 1)
            pool.affine_select(out=ident[:, :], in_=ident[:, :], compare_op=ALU.not_equal, fill=1.0,
                               base=0, pattern=[[-1, P]], channel_multiplier=1).then_inc(ident_ready, 1)
            pool.iota(part[:, :], pattern=[[0, 1]], base=0, channel_multiplier=1).then_inc(part_ready, 1)

            adapters = [pool.alloc_register(f"adapter{j}") for j in range(J)]

            def take_index(u, s, first=False):
                if not first:
                    pool.wait_ge(b_ready, u - 1)
                pool.tensor_copy(b_index_slot[s][:, :], b_index[:, bass.ds(u, 1)]).then_inc(b_index_copied, 1)

            def place_a(u, s, first=False):
                pool.load(adapters, ad_sb[0:1, bass.ds(u * J, J)])
                if not first:
                    pool.wait_ge(main_done, u - 1)
                    pool.wait_ge(b_index_copied, u + 1)
                for j in range(J):
                    slot = pool.snap(adapters[j], min_val=0, max_val=SLOTS - 1)
                    last = pool.tensor_copy(wa[:, :, :, j // HJ, a_columns(s, j)],
                                            a_split[:, bass.ds(slot * KC, KC), :, :])
                last.then_inc(a_ready, 1)

            def gather_b(s):
                pool.indirect_dma_start(
                    b_raw[s][:, :], None, lora_b.rearrange("s r o -> (s r) o"),
                    bass.IndirectOffsetOnAxis(ap=b_index_slot[s][:, 0:1], axis=0)).then_inc(b_gathered[s], 16)

            pool.wait_ge(b_index_ready, 1)
            take_index(0, 0, first=True)
            take_index(1, 1, first=True)
            pool.wait_ge(b_index_copied, 2)
            gather_b(0)
            gather_b(1)
            pool.wait_ge(a_split_ready, A_GROUPS)
            place_a(1, 1, first=True)
            with pool.Fori(1, TILES // 2) as i:
                for s in range(2):
                    u = 2 * i + s
                    take_index(u, s)
                    place_a(u, s)
                    gather_b(s)

        @block.scalar
        def _(act):
            for m in range(KM):
                act.dma_start(w_nat[:, :, m * TM:(m + 1) * TM],
                              w.rearrange("(k p) t -> p k t", p=P)[:, :, m * TM:(m + 1) * TM]).then_inc(w_loaded[m], 16)
            act.wait_ge(m_zero, 1)
            act.copy(m_blocks[1][:, :], m_blocks[0][:, :]).then_inc(m_zero, 1)

            adapters = [act.alloc_register(f"adapter{j}") for j in range(J)]
            conds = [act.alloc_register(f"cond{j}") for j in range(J)]

            def build_m(u, s, first=False):
                act.load(conds, cond_sb[0:1, bass.ds(u * J, J)])
                if not first:
                    act.wait_ge(x1_computed, u - 1)
                for j in range(J):
                    slot = act.snap(conds[j], min_val=0, max_val=S0 - 1)
                    q = slice(j * C, (j + 1) * C)
                    last = act.copy(m_blocks[s][q, q], w0_all[:, bass.ds(slot, 1), :])
                last.then_inc(m_ready, 1)

            def round_x1(u, s, first=False):
                act.wait_ge(x1_computed, u + 1)
                if not first:
                    act.wait_ge(main_done, u - 1)
                act.copy(x1_hi[s][:, :], x1_ps[s][:, :]).then_inc(x1_hi_ready, 1)

            def round_b(u, s, n, first=False):
                act.wait_ge(b_gathered[s], 16 * (n + 1))
                if not first:
                    act.wait_ge(lora_done, u - 1)
                act.copy(b_hi[s][:, :], b_raw[s][:, :]).then_inc(b_hi_ready, 1)

            def round_h(u, s, first=False, alone=False):
                act.wait_ge(main_done, u + 1)
                if not first:
                    act.wait_ge(ht_computed, u - 1)
                act.copy(h_split[s][:, :, 0, :].rearrange("p (a j) r -> p a j r", a=2),
                         h_of(s, alone)).then_inc(h_hi_ready, 1)

            act.wait_ge(cond_loaded, 16)
            act.wait_ge(w0_ready, 1)
            act.wait_ge(m_zero, 2)
            build_m(0, 0, first=True)
            build_m(1, 1, first=True)

            def round_w(k):
                act.wait_ge(wt_ps_ready, k + 1)
                act.copy(wa[:, k, 0, :, AC:AC + HALF],
                         y_ps[k // 2][:, k % 2, :].rearrange("p (a o) -> p a o", a=2)).then_inc(w_hi_ready, 1)

            def round_a(g):
                act.wait_ge(a_loaded[g], 16)
                act.copy(a_split[:, a_group(g), 0, :], a_raw[:, a_group(g), :]).then_inc(a_hi_ready, 1)

            round_w(0)
            round_w(1)
            round_x1(0, 0, first=True)
            round_w(2)
            round_w(3)
            round_x1(1, 1, first=True)
            for g in range(A_GROUPS):
                round_a(g)
            act.wait_ge(ad_loaded, 16)
            act.load(adapters, ad_sb[0:1, 0:J])
            act.wait_ge(a_split_ready, A_GROUPS)
            for j in range(J):
                slot = act.snap(adapters[j], min_val=0, max_val=SLOTS - 1)
                last = act.copy(wa[:, :, :, j // HJ, a_columns(0, j)], a_split[:, bass.ds(slot * KC, KC), :, :])
            last.then_inc(a0_ready, 1)
            build_m(2, 0)
            round_h(0, 0, first=True, alone=True)
            round_x1(2, 0)
            build_m(3, 1)
            round_h(1, 1, first=True, alone=True)
            round_b(0, 0, 0, first=True)
            round_x1(3, 1)
            round_b(1, 1, 0, first=True)
            build_m(4, 0)
            round_b(2, 0, 1)

            def step(u, s, n, more_x=True, more_m=True):
                round_h(u - 1, 1 - s)
                if more_x:
                    round_x1(u + 1, 1 - s)
                if more_m:
                    build_m(u + 2, s)
                round_b(u, s, n)

            with act.Fori(1, TILES // 2 - 2) as i:
                step(2 * i + 1, 1, i)
                step(2 * i + 2, 0, i + 1)
            step(TILES - 3, 1, TILES // 2 - 2)
            step(TILES - 2, 0, TILES // 2 - 1, more_m=False)
            step(TILES - 1, 1, TILES // 2 - 1, more_x=False, more_m=False)
            round_h(TILES - 1, 1, alone=True)

        @block.vector
        def _(dve):
            chained = [0]

            def link(ins):
                chained[0] += 1
                ins.then_inc(dve_chain, 1)
                dve.wait_ge(dve_chain, chained[0])

            nc.vector.memset(zeros[:, :], 0.0).then_inc(zeros_ready, 1)
            nc.vector.memset(m_blocks[0][:, :], 0.0).then_inc(m_zero, 1)
            nc.vector.memset(pick[:, :], 0.0)
            link(nc.vector.memset(own_mask[:, :], 0.0))
            for j in range(J):
                q = slice(j * C, (j + 1) * C)
                nc.vector.memset(own_mask[q, q], SCALING)
                last = nc.vector.memset(pick[q, j:j + 1], float(R))
            link(last)
            def row_indices():
                dve.wait_ge(part_ready, 1)
                link(nc.vector.tensor_single_scalar(r_int[:, :], part[:, :], R - 1, ALU.bitwise_and))
                link(nc.vector.tensor_copy(r_of_p[:, :], r_int[:, :]))
                dve.wait_ge(ad_loaded, 16)
                link(nc.vector.tensor_tensor(ad_pick[:, :, :], ad_sb[:, :].rearrange("p (u j) -> p u j", j=J),
                                             pick[:, :].rearrange("p (a j) -> p a j", a=1).broadcast_to([P, TILES, J]), ALU.mult))
                link(nc.vector.reduce_sum(ad_row[:, :], ad_pick[:, :, :], AX_X))
                nc.vector.tensor_scalar(b_index[:, :], ad_row[:, :], r_of_p[:, 0:1], None,
                                        ALU.add).then_inc(b_index_ready, 1)

            dve.wait_ge(ident_ready, 1)
            dve.wait_ge(w0_loaded, 16)
            nc.vector.tensor_tensor(w0_all[:, :, :], w0_all[:, :, :],
                                    ident[0:C, 0:C].rearrange("p (a d) -> p a d", a=1).broadcast_to([C, S0, C]),
                                    ALU.add).then_inc(w0_ready, 1)
            for m in range(KM):
                dve.wait_ge(w_loaded[m], 16)
                for k in range(2 * m, 2 * m + 2):
                    last = nc.vector.tensor_tensor(w_nat[:, k, k * P:(k + 1) * P], w_nat[:, k, k * P:(k + 1) * P],
                                                   ident[:, :], ALU.add)
                last.then_inc(w_plus_i, 1)
            row_indices()

            def rest_w(k):
                dve.wait_ge(w_hi_ready, k + 1)
                nc.vector.tensor_tensor(wa[:, k, 1, :, AC:AC + HALF],
                                        y_ps[k // 2][:, k % 2, :].rearrange("p (a o) -> p a o", a=2),
                                        wa[:, k, 0, :, AC:AC + HALF], ALU.subtract).then_inc(w_ready, 1)

            def rest_a(g):
                dve.wait_ge(a_hi_ready, g + 1)
                nc.vector.tensor_tensor(a_split[:, a_group(g), 1, :], a_raw[:, a_group(g), :],
                                        a_split[:, a_group(g), 0, :], ALU.subtract).then_inc(a_split_ready, 1)

            def rest_x1(u, s):
                dve.wait_ge(x1_hi_ready, u + 1)
                nc.vector.tensor_tensor(x1_lo[s][:, :], x1_ps[s][:, :], x1_hi[s][:, :],
                                        ALU.subtract).then_inc(x1_ready, 1)

            def rest_b(u, s):
                dve.wait_ge(b_hi_ready, u + 1)
                nc.vector.tensor_tensor(b_lo[s][:, :], b_raw[s][:, :], b_hi[s][:, :],
                                        ALU.subtract).then_inc(b_ready, 1)

            def rest_h(u, s, alone=False):
                dve.wait_ge(h_hi_ready, u + 1)
                nc.vector.tensor_tensor(
                    h_split[s][:, :, 1, :].rearrange("p (a j) r -> p a j r", a=2),
                    h_of(s, alone), h_split[s][:, :, 0, :].rearrange("p (a j) r -> p a j r", a=2),
                    ALU.subtract).then_inc(h_ready, 1)

            def mask_ht(u, s, first=False):
                dve.wait_ge(ht_computed, u + 1)
                if not first:
                    dve.wait_ge(lora_done, u - 1)
                nc.vector.tensor_tensor(ht_sb[s][:, :], ht_ps[s][:, 0:P], own_mask[:, :],
                                        ALU.mult).then_inc(ht_ready, 1)

            def finish_y(u, s, n, first=False):
                dve.wait_ge(lora_done, u + 1)
                if not first:
                    dve.wait_ge(y_stored[s], 16 * n)
                nc.vector.tensor_tensor(
                    y_sb[s][:, :].rearrange("p (a o) -> p a o", a=2),
                    y_ps[s][:, :, Y_PS[s]:Y_PS[s] + HALF],
                    bias_sb[:, :].rearrange("p (a o) -> p a o", a=2), ALU.add).then_inc(y_ready, 1)

            rest_w(0)
            rest_w(1)
            rest_x1(0, 0)
            rest_w(2)
            rest_w(3)
            rest_x1(1, 1)
            for g in range(A_GROUPS):
                rest_a(g)
            dve.wait_ge(bias_loaded, 16)

            rest_h(0, 0, alone=True)
            mask_ht(0, 0, first=True)
            rest_x1(2, 0)
            rest_b(0, 0)
            rest_h(1, 1, alone=True)
            mask_ht(1, 1, first=True)
            rest_x1(3, 1)
            rest_b(1, 1)
            finish_y(0, 0, 0, first=True)
            finish_y(1, 1, 0, first=True)
            rest_b(2, 0)

            def step(u, s, n, more_x=True):
                rest_h(u - 1, 1 - s)
                mask_ht(u - 1, 1 - s)
                if more_x:
                    rest_x1(u + 1, 1 - s)
                rest_b(u, s)
                finish_y(u - 1, 1 - s, n)

            with dve.Fori(1, TILES // 2 - 1) as i:
                step(2 * i + 1, 1, i)
                step(2 * i + 2, 0, i)
            step(TILES - 1, 1, TILES // 2 - 1, more_x=False)
            rest_h(TILES - 1, 1, alone=True)
            mask_ht(TILES - 1, 1)
            finish_y(TILES - 1, 1, TILES // 2 - 1)

        @block.tensor
        def _(pe):
            def x1_of(u, s, n, first=False):
                pe.wait_ge(x_loaded[s], 16 * (n + 1))
                pe.wait_ge(m_ready, u + 1)
                if not first:
                    pe.wait_ge(x1_ready, u - 1)
                for k in range(KC):
                    last = nc.tensor.matmul(x1_ps[s][:, k * P:(k + 1) * P], x_sb[s][:, chunk_of_t(k)],
                                            m_blocks[s][:, :], start=True, stop=True)
                last.then_inc(x1_computed, 1)

            def products(s, k, target, weights):
                for lo_x, lo_w in ((0, 0), (0, 1), (1, 0)):
                    last = nc.tensor.matmul(
                        target, (x1_lo if lo_x else x1_hi)[s][:, k * P:(k + 1) * P], weights(lo_w),
                        start=(k == 0 and not lo_x and not lo_w), stop=(k == KC - 1 and lo_x == 1),
                        skip_group_check=True)
                return last

            def main_chunk(s, k, with_h=True):
                at, n, to = (MOV[s], NW, 0) if with_h else (AC, HALF, Y_PS[s])
                for half in range(2):
                    last = products(s, k, y_ps[s][:, half, to:to + n],
                                    lambda lo_w: wa[:, k, lo_w, half, at:at + n])
                return last

            def wait_main(u, s, first=False):
                pe.wait_ge(x1_ready, u + 1)
                if not first:
                    pe.wait_ge(y_ready, u - 1)

            def wait_a(u):
                pe.wait_ge(a_ready, u)

            def h_alone(s):
                for k in range(KC):
                    last = products(s, k, ht_ps[s][:, P:P + 2 * AC],
                                    lambda lo_w: wa[:, k, lo_w, :, A_AT[s]:A_AT[s] + AC])
                return last

            def transpose_h(u, s):
                pe.wait_ge(h_ready, u + 1)
                nc.tensor.transpose(ht_ps[s][:, 0:P], h_split[s][:, :, :, :].rearrange("p j e r -> p (j e r)").bitcast(F32),
                                    ident[:, :]).then_inc(ht_computed, 1)

            def lora(u, s):
                pe.wait_ge(ht_ready, u + 1)
                pe.wait_ge(b_ready, u + 1)
                for half in range(2):
                    for b_part in (b_hi, b_lo):
                        last = nc.tensor.matmul(
                            y_ps[s][:, half, Y_PS[s]:Y_PS[s] + HALF], ht_sb[s][:, :],
                            b_part[s][:, half * HALF:(half + 1) * HALF], start=False, stop=True,
                            skip_group_check=True)
                last.then_inc(lora_done, 1)

            pe.wait_ge(zeros_ready, 1)
            for _ in range(WARM_UP):
                nc.tensor.matmul(ht_ps[0][:, :], zeros[:, 0:P], zeros[:, :], start=True, stop=True)

            def transpose_w(m):
                pe.wait_ge(w_plus_i, m + 1)
                for k in range(2 * m, 2 * m + 2):
                    for ok in range(KC):
                        last = nc.tensor.transpose(y_ps[m][:, k % 2, ok * P:(ok + 1) * P],
                                                   w_nat[:, ok, chunk_of_t(k)], ident[:, :])
                    last.then_inc(wt_ps_ready, 1)

            transpose_w(0)
            x1_of(0, 0, 0, first=True)
            transpose_w(1)
            x1_of(1, 1, 0, first=True)
            pe.wait_ge(w_ready, KC)
            for u in range(2):
                wait_main(u, u, first=True)
                for k in range(KC):
                    main_chunk(u, k, with_h=False)
            pe.wait_ge(a0_ready, 1)
            h_alone(0).then_inc(main_done, 1)
            x1_of(2, 0, 1)
            wait_a(1)
            h_alone(1).then_inc(main_done, 1)
            transpose_h(0, 0)
            x1_of(3, 1, 1)
            lora(0, 0)
            transpose_h(1, 1)
            lora(1, 1)
            wait_main(2, 0)
            wait_a(2)
            for k in range(KC):
                last = main_chunk(0, k)
            last.then_inc(main_done, 1)
            x1_of(4, 0, 2)

            def step(u, s, n_x=None):
                wait_main(u, s)
                wait_a(u)
                main_chunk(s, 0)
                transpose_h(u - 1, 1 - s)
                main_chunk(s, 1)
                main_chunk(s, 2)
                lora(u - 1, 1 - s)
                main_chunk(s, 3).then_inc(main_done, 1)
                if n_x is not None:
                    x1_of(u + 2, s, n_x)

            with pe.Fori(1, TILES // 2 - 2) as i:
                step(2 * i + 1, 1, i + 1)
                step(2 * i + 2, 0, i + 2)
            step(TILES - 3, 1, TILES // 2 - 1)
            step(TILES - 2, 0)
            u = TILES - 1
            wait_main(u, 1)
            wait_a(u)
            main_chunk(1, 0, with_h=False)
            transpose_h(u - 1, 0)
            h_alone(1).then_inc(main_done, 1)
            main_chunk(1, 1, with_h=False)
            lora(u - 1, 0)
            main_chunk(1, 2, with_h=False)
            transpose_h(u, 1)
            main_chunk(1, 3, with_h=False)
            lora(u, 1)


_INS = ["x", "itok_B_0_15", "itok_B_0_23", "L0_cond_weights", "L1_cond_W", "L1_cond_b",
        "L1_cond_lora_As", "L1_cond_lora_Bs"]


def kernel(**inputs):
    import numpy as _np
    import concourse.bacc as _bacc
    from concourse import mybir as _mybir
    from concourse.bass_utils import run_bass_kernel_spmd as _run

    nc = _bacc.Bacc("TRN2", target_bir_lowering=False, num_devices=1)
    arrays, args = {}, []
    for name in _INS:
        a = _np.ascontiguousarray(inputs[name])
        arrays[f"in_{name}"] = a
        args.append(nc.dram_tensor(f"in_{name}", a.shape, _mybir.dt.from_np(a.dtype), kind="ExternalInput").ap())
    shape = inputs["x"].shape
    args.append(nc.dram_tensor("out", shape, _mybir.dt.float32, kind="ExternalOutput").ap())
    lora_residual_program(nc, *args)
    r = _run(nc, [arrays], core_ids=[0])
    return r.results[0]["out"]
```

```python
from contextlib import ExitStack

import concourse.bass as bass
from concourse import mybir

F32 = mybir.dt.float32
F32R = mybir.dt.float32r
BF16 = mybir.dt.bfloat16
I32 = mybir.dt.int32
U32 = mybir.dt.uint32
ALU = mybir.AluOpType

P = 128
ALPHA = 32


def lora_residual_program(nc, x, cond, adapter, w0, w, bias, lora_a, lora_b, out):
    B, C, T = x.shape
    S0 = w0.shape[0]
    SLOTS, _, R = lora_a.shape
    O = w.shape[0]
    SCALING = float(ALPHA // R)
    J = P // C
    TILES = B // J
    KC = T // P
    WARM_UP = 9
    HALF = O // 2
    HJ = J // 2
    AC = HJ * R
    NW = AC + HALF
    WROW = AC + HALF + 2 * AC
    A_AT = (0, AC + HALF)
    MOV = (0, AC)
    H_PS = (0, HALF)
    Y_PS = (AC, 0)
    assert C == 32 and 2 * R == 32 and J == 4 and O == T == 512 and TILES % 2 == 0

    x_rows = x.rearrange("b c t -> (b c) t")
    out_rows = out.rearrange("b c t -> (b c) t")

    with ExitStack() as ctx:
        def sb(name, shape, dt):
            return ctx.enter_context(nc.sbuf_tensor(name, shape, dt))

        def sem(name):
            return ctx.enter_context(nc.semaphore(name))

        ident = sb("ident", [P, P], F32)
        own_mask = sb("own_mask", [P, P], F32)
        pick = sb("pick", [P, J], F32)
        part = sb("part", [P, 1], I32)
        r_int = sb("r_int", [P, 1], I32)
        r_of_p = sb("r_of_p", [P, 1], F32)
        zeros = sb("zeros", [P, P], BF16)
        cond_sb = sb("cond_sb", [1, B], I32)
        ad_sb = sb("ad_sb", [P, B], I32)
        ad_f = sb("ad_f", [P, B], F32)
        ad_pick = sb("ad_pick", [P, TILES, J], F32)
        ad_row = sb("ad_row", [P, TILES], F32)
        b_index = sb("b_index", [P, TILES], U32)
        b_index_slot = [sb(f"b_index_slot{s}", [P, 1], U32) for s in range(2)]
        w0_all = sb("w0_all", [C, S0, C], F32)
        m_blocks = [sb(f"m_blocks{s}", [P, P], F32) for s in range(2)]
        w_nat = sb("w_nat", [P, O // P, T], F32)
        wa = sb("wa", [P, KC, 2, 2, WROW], F32R)
        a_raw = [sb(f"a_raw{s}", [P, J, KC, R], F32) for s in range(2)]
        bias_sb = sb("bias_sb", [P, O], F32)
        b_raw = [sb(f"b_raw{s}", [P, O], F32) for s in range(2)]
        b_hi = [sb(f"b_hi{s}", [P, O], F32R) for s in range(2)]
        b_lo = [sb(f"b_lo{s}", [P, O], F32R) for s in range(2)]
        x_sb = [sb(f"x_sb{s}", [P, T], F32) for s in range(2)]
        x1_hi = [sb(f"x1_hi{s}", [P, T], F32R) for s in range(2)]
        x1_lo = [sb(f"x1_lo{s}", [P, T], F32R) for s in range(2)]
        h_split = [sb(f"h_split{s}", [P, J, 2, R], F32R) for s in range(2)]
        ht_sb = [sb(f"ht_sb{s}", [P, P], F32R) for s in range(2)]
        y_sb = [sb(f"y_sb{s}", [P, O], F32) for s in range(2)]

        y_ps = [ctx.enter_context(nc.psum_tensor(f"y_ps{s}", [P, 2, 512], F32)) for s in range(2)]
        x1_ps = [ctx.enter_context(nc.psum_tensor(f"x1_ps{s}", [P, T], F32)) for s in range(2)]
        ht_ps = [ctx.enter_context(nc.psum_tensor(f"ht_ps{s}", [P, 512], F32)) for s in range(2)]

        cond_loaded = sem("cond_loaded")
        ad_loaded = sem("ad_loaded")
        w0_loaded = sem("w0_loaded")
        w_loaded = [sem(f"w_loaded{half}") for half in range(2)]
        a_loaded = [[sem(f"a_loaded{s}_half{half}") for half in range(2)] for s in range(2)]
        bias_loaded = sem("bias_loaded")
        x_loaded = [sem(f"x_loaded{s}") for s in range(2)]
        b_gathered = [sem(f"b_gathered{s}") for s in range(2)]
        y_stored = [sem(f"y_stored{s}") for s in range(2)]
        ident_zero = sem("ident_zero")
        ident_ready = sem("ident_ready")
        zeros_ready = sem("zeros_ready")
        m_zero = sem("m_zero")
        mask_zero = sem("mask_zero")
        mask_ready = sem("mask_ready")
        pool_chain = sem("pool_chain")
        part_ready = sem("part_ready")
        r_int_ready = sem("r_int_ready")
        r_ready = sem("r_ready")
        w0_ready = sem("w0_ready")
        w_plus_i = sem("w_plus_i")
        wt_ps_ready = sem("wt_ps_ready")
        w_hi_ready = sem("w_hi_ready")
        w_ready = sem("w_ready")
        a_hi_ready = sem("a_hi_ready")
        a_ready = sem("a_ready")
        b_index_ready = sem("b_index_ready")
        b_index_copied = sem("b_index_copied")
        m_ready = sem("m_ready")
        b_hi_ready = sem("b_hi_ready")
        b_ready = sem("b_ready")
        x1_computed = sem("x1_computed")
        x1_hi_ready = sem("x1_hi_ready")
        x1_ready = sem("x1_ready")
        main_done = sem("main_done")
        h_hi_ready = sem("h_hi_ready")
        h_ready = sem("h_ready")
        ht_computed = sem("ht_computed")
        ht_ready = sem("ht_ready")
        lora_done = sem("lora_done")
        y_ready = sem("y_ready")


        block = ctx.enter_context(nc.Block())

        def a_half(s, half):
            return a_raw[s][:, half * HJ:(half + 1) * HJ, :, :].rearrange("p j k r -> p k j r")

        def a_place(s, half, lo, last_tile=False):
            row, at = (0, A_AT[s] + half * AC) if last_tile else (half, A_AT[s])
            return wa[:, :, lo, row, at:at + AC].rearrange("p k (j r) -> p k j r", j=HJ)

        def h_of(s, last_tile=False):
            if last_tile:
                return y_ps[s][:, 0, H_PS[s]:H_PS[s] + 2 * AC].rearrange("p (a j r) -> p a j r", a=2, j=HJ)
            return y_ps[s][:, :, H_PS[s]:H_PS[s] + AC].rearrange("p a (j r) -> p a j r", j=HJ)

        def chunk_of_t(k):
            return slice(k, T, KC)

        def piece_ps(q):
            return y_ps[q // 2][:, q % 2, :].rearrange("p (k o) -> p k o", k=2)

        def piece_of_w(q, lo):
            k = 2 * (q % 2)
            return wa[:, k:k + 2, lo, q // 2, AC:AC + HALF]

        @block.sync
        def _(sp):
            def load_w(half):
                sp.dma_start(w_nat[:, 2 * half:2 * half + 2, :],
                             w.rearrange("(c p) t -> p c t", p=P)[:, 2 * half:2 * half + 2, :]).then_inc(w_loaded[half], 16)

            def load_x(u, s):
                sp.dma_start(x_sb[s][:, :], x_rows[bass.ds(u * P, P), :]).then_inc(x_loaded[s], 16)

            def store_y(u, s):
                sp.wait_ge(y_ready, u + 1)
                sp.dma_start(out_rows[bass.ds(u * P, P), :], y_sb[s][:, :]).then_inc(y_stored[s], 16)

            adapters = [sp.alloc_register(f"adapter{j}") for j in range(J)]

            def load_a(u, s, first=False):
                if not first:
                    sp.wait_ge(a_ready, 2 * u - 2)
                sp.load(adapters, ad_sb[0:1, bass.ds(u * J, J)])
                for j in range(J):
                    slot = sp.snap(adapters[j], min_val=0, max_val=SLOTS - 1)
                    sp.dma_start(a_raw[s][:, j:j + 1, :, :].rearrange("p j k r -> p j (k r)"),
                                 lora_a[bass.ds(slot, 1)].rearrange("s (p k) r -> p s (k r)", k=KC)
                                 ).then_inc(a_loaded[s][j // HJ], 16)

            load_w(0)
            sp.dma_start(w0_all[:, :, :], w0.rearrange("s c d -> c s d")).then_inc(w0_loaded, 16)
            load_x(0, 0)
            load_w(1)
            load_x(1, 1)
            sp.wait_ge(ad_loaded, 16)
            load_a(0, 0, first=True)
            load_a(1, 1, first=True)
            sp.wait_ge(x1_computed, 1)
            load_x(2, 0)
            sp.wait_ge(x1_computed, 2)
            load_x(3, 1)
            sp.dma_start(bias_sb[:, :], bias.rearrange("(a o) -> a o", a=1).broadcast_to([P, O])).then_inc(bias_loaded, 16)
            load_a(2, 0)
            with sp.Fori(0, TILES // 2 - 2) as i:
                for s in range(2):
                    u = 2 * i + s
                    load_a(u + 3, 1 - s)
                    sp.wait_ge(x1_computed, u + 3)
                    load_x(u + 4, s)
                    store_y(u, s)
            load_a(TILES - 1, 1)
            for u in range(TILES - 4, TILES - 1):
                store_y(u, u % 2)
            u = TILES - 1
            for half in range(2):
                cols = slice(half * HALF, (half + 1) * HALF)
                sp.wait_ge(y_ready, u + 1 + half)
                sp.dma_start(out_rows[u * P:(u + 1) * P, cols], y_sb[1][:, cols]).then_inc(y_stored[1], 16)
            sp.wait_ge(y_stored[0], 16 * (TILES // 2))
            sp.wait_ge(y_stored[1], 16 * (TILES // 2 + 1))

        @block.gpsimd
        def _(pool):
            pool.memset(ident[:, :], 0.0).then_inc(ident_zero, 1)
            pool.iota(part[:, :], pattern=[[0, 1]], base=0, channel_multiplier=1).then_inc(part_ready, 1)
            pool.wait_ge(ident_zero, 1)
            pool.affine_select(out=ident[:, :], in_=ident[:, :], compare_op=ALU.not_equal, fill=1.0,
                               base=0, pattern=[[-1, P]], channel_multiplier=1).then_inc(ident_ready, 1)

            chained = [0]

            def link(ins):
                chained[0] += 1
                ins.then_inc(pool_chain, 1)
                pool.wait_ge(pool_chain, chained[0])

            link(pool.memset(pick[:, :], 0.0))
            for j in range(J):
                link(pool.memset(pick[j * C:(j + 1) * C, j:j + 1], float(R)))
            pool.wait_ge(ad_loaded, 16)
            link(pool.tensor_copy(ad_f[:, :], ad_sb[:, :]))
            link(pool.tensor_tensor(ad_pick[:, :, :], ad_f[:, :].rearrange("p (u j) -> p u j", j=J),
                                    pick[:, :].rearrange("p (a j) -> p a j", a=1).broadcast_to([P, TILES, J]), ALU.mult))
            for half in range(2):
                link(pool.tensor_tensor(ad_pick[:, :, half], ad_pick[:, :, half], ad_pick[:, :, half + 2], ALU.add))
            link(pool.tensor_tensor(ad_row[:, :], ad_pick[:, :, 0], ad_pick[:, :, 1], ALU.add))
            pool.wait_ge(r_ready, 1)
            pool.tensor_scalar(b_index[:, :], ad_row[:, :], r_of_p[:, 0:1], None, ALU.add).then_inc(b_index_ready, 1)

            def take_index(u, s, n=None):
                if n is not None:
                    pool.wait_ge(b_gathered[s], 16 * n)
                pool.tensor_copy(b_index_slot[s][:, :], b_index[:, bass.ds(u, 1)]).then_inc(b_index_copied, 1)

            def gather_b(s):
                pool.indirect_dma_start(
                    b_raw[s][:, :], None, lora_b.rearrange("s r o -> (s r) o"),
                    bass.IndirectOffsetOnAxis(ap=b_index_slot[s][:, 0:1], axis=0)).then_inc(b_gathered[s], 16)

            pool.wait_ge(b_index_ready, 1)
            take_index(0, 0)
            take_index(1, 1)
            pool.wait_ge(b_index_copied, 2)
            gather_b(0)
            gather_b(1)
            take_index(2, 0, 1)

            def step(u, s, n):
                pool.wait_ge(b_index_copied, u)
                pool.wait_ge(b_ready, u - 2)
                take_index(u, s, n)
                gather_b(1 - s)

            with pool.Fori(1, TILES // 2 - 1) as i:
                step(2 * i + 1, 1, i)
                step(2 * i + 2, 0, i + 1)
            step(TILES - 1, 1, TILES // 2 - 1)
            pool.wait_ge(b_index_copied, TILES)
            pool.wait_ge(b_ready, TILES - 2)
            gather_b(1)

        @block.scalar
        def _(act):
            act.dma_start(ad_sb[:, :], adapter.rearrange("(a b) -> a b", a=1).broadcast_to([P, B])).then_inc(ad_loaded, 16)
            act.dma_start(cond_sb[:, :], cond.rearrange("(a b) -> a b", a=1)).then_inc(cond_loaded, 16)
            act.wait_ge(m_zero, 1)
            act.copy(m_blocks[1][:, :], m_blocks[0][:, :]).then_inc(m_zero, 1)

            conds = [act.alloc_register(f"cond{j}") for j in range(J)]

            def build_m(u, s, first=False):
                act.load(conds, cond_sb[0:1, bass.ds(u * J, J)])
                slots = [act.snap(conds[j], min_val=0, max_val=S0 - 1) for j in range(J)]
                if first:
                    act.wait_ge(w0_ready, 1)
                else:
                    act.wait_ge(x1_computed, u - 1)
                for j in range(J):
                    q = slice(j * C, (j + 1) * C)
                    last = act.copy(m_blocks[s][q, q], w0_all[:, bass.ds(slots[j], 1), :])
                last.then_inc(m_ready, 1)

            def round_x1(u, s, first=False):
                act.wait_ge(x1_computed, u + 1)
                if not first:
                    act.wait_ge(main_done, u - 1)
                act.copy(x1_hi[s][:, :], x1_ps[s][:, :]).then_inc(x1_hi_ready, 1)

            def round_b(u, s, n, first=False):
                act.wait_ge(b_gathered[s], 16 * (n + 1))
                if not first:
                    act.wait_ge(lora_done, u - 1)
                act.copy(b_hi[s][:, :], b_raw[s][:, :]).then_inc(b_hi_ready, 1)

            def round_h(u, s, first=False, last_tile=False):
                act.wait_ge(main_done, u + 1)
                if not first:
                    act.wait_ge(ht_computed, u - 1)
                act.copy(h_split[s][:, :, 0, :].rearrange("p (a j) r -> p a j r", a=2),
                         h_of(s, last_tile)).then_inc(h_hi_ready, 1)

            def round_w(q):
                act.wait_ge(wt_ps_ready, q + 1)
                act.copy(piece_of_w(q, 0), piece_ps(q)).then_inc(w_hi_ready, 1)

            def round_a(u, s, n, first=False, last_tile=False):
                if not first:
                    act.wait_ge(main_done, u - 1)
                for half in range(2):
                    act.wait_ge(a_loaded[s][half], 16 * HJ * (n + 1))
                    act.copy(a_place(s, half, 0, last_tile), a_half(s, half)).then_inc(a_hi_ready, 1)

            act.wait_ge(cond_loaded, 16)
            act.wait_ge(m_zero, 2)
            build_m(0, 0, first=True)
            round_w(0)
            round_w(1)
            build_m(1, 1, first=True)
            round_x1(0, 0, first=True)
            round_a(0, 0, 0, first=True)
            round_w(2)
            round_w(3)
            round_x1(1, 1, first=True)
            build_m(2, 0)
            round_a(1, 1, 0, first=True)
            round_b(0, 0, 0, first=True)

            def step(u, s, n, n_next=None, more_m=True, first_h=False, first_b=False, last_a=False):
                round_h(u - 1, 1 - s, first_h)
                if n_next is not None:
                    round_x1(u + 1, 1 - s)
                    round_a(u + 1, 1 - s, n_next, last_tile=last_a)
                if more_m:
                    build_m(u + 2, s)
                round_b(u, s, n, first_b)

            step(1, 1, 0, 1, first_h=True, first_b=True)
            step(2, 0, 1, 1, first_h=True)
            with act.Fori(1, TILES // 2 - 2) as i:
                step(2 * i + 1, 1, i, i + 1)
                step(2 * i + 2, 0, i + 1, i + 1)
            step(TILES - 3, 1, TILES // 2 - 2, TILES // 2 - 1)
            step(TILES - 2, 0, TILES // 2 - 1, TILES // 2 - 1, more_m=False, last_a=True)
            step(TILES - 1, 1, TILES // 2 - 1, more_m=False)
            round_h(TILES - 1, 1, last_tile=True)

        @block.vector
        def _(dve):
            nc.vector.memset(zeros[:, :], 0.0).then_inc(zeros_ready, 1)
            nc.vector.memset(m_blocks[0][:, :], 0.0).then_inc(m_zero, 1)
            nc.vector.memset(own_mask[:, :], 0.0).then_inc(mask_zero, 1)
            dve.wait_ge(mask_zero, 1)
            for j in range(J):
                q = slice(j * C, (j + 1) * C)
                last = nc.vector.memset(own_mask[q, q], SCALING)
            last.then_inc(mask_ready, 1)
            dve.wait_ge(part_ready, 1)
            nc.vector.tensor_single_scalar(r_int[:, :], part[:, :], R - 1, ALU.bitwise_and).then_inc(r_int_ready, 1)
            dve.wait_ge(r_int_ready, 1)
            nc.vector.tensor_copy(r_of_p[:, :], r_int[:, :]).then_inc(r_ready, 1)
            dve.wait_ge(ident_ready, 1)

            def add_identity(half):
                dve.wait_ge(w_loaded[half], 16)
                for c in range(2 * half, 2 * half + 2):
                    nc.vector.tensor_tensor(w_nat[:, c, c * P:(c + 1) * P], w_nat[:, c, c * P:(c + 1) * P],
                                            ident[:, :], ALU.add).then_inc(w_plus_i, 1)

            add_identity(0)
            dve.wait_ge(w0_loaded, 16)
            nc.vector.tensor_tensor(w0_all[:, :, :], w0_all[:, :, :],
                                    ident[0:C, 0:C].rearrange("p (a d) -> p a d", a=1).broadcast_to([C, S0, C]),
                                    ALU.add).then_inc(w0_ready, 1)
            add_identity(1)

            def rest_w(q):
                dve.wait_ge(w_hi_ready, q + 1)
                nc.vector.tensor_tensor(piece_of_w(q, 1), piece_ps(q), piece_of_w(q, 0),
                                        ALU.subtract).then_inc(w_ready, 1)

            def rest_a(u, s, last_tile=False):
                for half in range(2):
                    dve.wait_ge(a_hi_ready, 2 * u + half + 1)
                    nc.vector.tensor_tensor(a_place(s, half, 1, last_tile), a_half(s, half),
                                            a_place(s, half, 0, last_tile), ALU.subtract).then_inc(a_ready, 1)

            def rest_x1(u, s):
                dve.wait_ge(x1_hi_ready, u + 1)
                nc.vector.tensor_tensor(x1_lo[s][:, :], x1_ps[s][:, :], x1_hi[s][:, :],
                                        ALU.subtract).then_inc(x1_ready, 1)

            def rest_b(u, s):
                dve.wait_ge(b_hi_ready, u + 1)
                nc.vector.tensor_tensor(b_lo[s][:, :], b_raw[s][:, :], b_hi[s][:, :],
                                        ALU.subtract).then_inc(b_ready, 1)

            def rest_h(u, s, last_tile=False):
                dve.wait_ge(h_hi_ready, u + 1)
                nc.vector.tensor_tensor(
                    h_split[s][:, :, 1, :].rearrange("p (a j) r -> p a j r", a=2),
                    h_of(s, last_tile), h_split[s][:, :, 0, :].rearrange("p (a j) r -> p a j r", a=2),
                    ALU.subtract).then_inc(h_ready, 1)

            def mask_ht(u, s, first=False):
                dve.wait_ge(ht_computed, u + 1)
                if not first:
                    dve.wait_ge(lora_done, u - 1)
                nc.vector.tensor_tensor(ht_sb[s][:, :], ht_ps[s][:, 0:P], own_mask[:, :],
                                        ALU.mult).then_inc(ht_ready, 1)

            def finish_y(u, s, n, first=False):
                dve.wait_ge(lora_done, u + 1)
                if not first:
                    dve.wait_ge(y_stored[s], 16 * n)
                nc.vector.tensor_tensor(
                    y_sb[s][:, :].rearrange("p (a o) -> p a o", a=2),
                    y_ps[s][:, :, Y_PS[s]:Y_PS[s] + HALF],
                    bias_sb[:, :].rearrange("p (a o) -> p a o", a=2), ALU.add).then_inc(y_ready, 1)

            def finish_last_y():
                s, n = 1, TILES // 2 - 1
                dve.wait_ge(y_stored[s], 16 * n)
                for half in range(2):
                    dve.wait_ge(lora_done, TILES + half)
                    cols = slice(half * HALF, (half + 1) * HALF)
                    nc.vector.tensor_tensor(y_sb[s][:, cols], y_ps[s][:, half, Y_PS[s]:Y_PS[s] + HALF],
                                            bias_sb[:, cols], ALU.add).then_inc(y_ready, 1)

            rest_w(0)
            rest_w(1)
            rest_x1(0, 0)
            rest_a(0, 0)
            rest_w(2)
            rest_w(3)
            rest_x1(1, 1)
            rest_a(1, 1)
            rest_b(0, 0)
            dve.wait_ge(mask_ready, 1)
            dve.wait_ge(bias_loaded, 16)

            def step(u, s, n, first=False, last_a=False):
                rest_h(u - 1, 1 - s)
                mask_ht(u - 1, 1 - s, first)
                rest_x1(u + 1, 1 - s)
                rest_a(u + 1, 1 - s, last_a)
                finish_y(u - 1, 1 - s, n, first)
                rest_b(u, s)

            step(1, 1, 0, first=True)
            step(2, 0, 0, first=True)
            with dve.Fori(1, TILES // 2 - 2) as i:
                step(2 * i + 1, 1, i)
                step(2 * i + 2, 0, i)
            step(TILES - 3, 1, TILES // 2 - 2)
            step(TILES - 2, 0, TILES // 2 - 2, last_a=True)
            u = TILES - 1
            rest_h(u - 1, 0)
            mask_ht(u - 1, 0)
            rest_b(u, 1)
            rest_h(u, 1, last_tile=True)
            finish_y(u - 1, 0, TILES // 2 - 1)
            mask_ht(u, 1)
            finish_last_y()

        @block.tensor
        def _(pe):
            def x1_of(u, s, n, first=False):
                pe.wait_ge(x_loaded[s], 16 * (n + 1))
                pe.wait_ge(m_ready, u + 1)
                if not first:
                    pe.wait_ge(x1_ready, u - 1)
                for k in range(KC):
                    last = nc.tensor.matmul(x1_ps[s][:, k * P:(k + 1) * P], x_sb[s][:, chunk_of_t(k)],
                                            m_blocks[s][:, :], start=True, stop=True)
                last.then_inc(x1_computed, 1)

            def products(s, k, target, weights):
                for lo_x, lo_w in ((0, 0), (0, 1), (1, 0)):
                    last = nc.tensor.matmul(
                        target, (x1_lo if lo_x else x1_hi)[s][:, k * P:(k + 1) * P], weights(lo_w),
                        start=(k == 0 and not lo_x and not lo_w), stop=(k == KC - 1 and lo_x == 1),
                        skip_group_check=True)
                return last

            def main_chunk(s, k, halves=range(2)):
                at, n, to = MOV[s], NW, 0
                for half in halves:
                    last = products(s, k, y_ps[s][:, half, to:to + n],
                                    lambda lo_w: wa[:, k, lo_w, half, at:at + n])
                return last

            def wait_main(u, s, first=False):
                pe.wait_ge(x1_ready, u + 1)
                pe.wait_ge(a_ready, 2 * u + 2)
                if not first:
                    pe.wait_ge(y_ready, u - 1)

            def transpose_h(u, s):
                pe.wait_ge(h_ready, u + 1)
                nc.tensor.transpose(ht_ps[s][:, 0:P], h_split[s][:, :, :, :].rearrange("p j e r -> p (j e r)").bitcast(F32),
                                    ident[:, :]).then_inc(ht_computed, 1)

            def lora(u, s, by_halves=False):
                pe.wait_ge(ht_ready, u + 1)
                pe.wait_ge(b_ready, u + 1)
                for half in range(2):
                    for b_part in (b_hi, b_lo):
                        last = nc.tensor.matmul(
                            y_ps[s][:, half, Y_PS[s]:Y_PS[s] + HALF], ht_sb[s][:, :],
                            b_part[s][:, half * HALF:(half + 1) * HALF], start=False, stop=True,
                            skip_group_check=True)
                    if by_halves or half == 1:
                        last.then_inc(lora_done, 1)

            pe.wait_ge(zeros_ready, 1)
            for _ in range(WARM_UP):
                nc.tensor.matmul(ht_ps[0][:, :].rearrange("p (a c) -> p a c", c=P), zeros[:, :],
                                 zeros[:, :].rearrange("p (a c) -> p a c", a=1).broadcast_to([P, 512 // P, P]),
                                 start=True, stop=True)

            def transpose_w(half):
                for c in range(2):
                    pe.wait_ge(w_plus_i, 2 * half + c + 1)
                    for q in range(2 * half, 2 * half + 2):
                        for k in range(2):
                            last = nc.tensor.transpose(piece_ps(q)[:, k, c * P:(c + 1) * P],
                                                       w_nat[:, 2 * half + c, chunk_of_t(2 * (q % 2) + k)],
                                                       ident[:, :])
                        if c == 1:
                            last.then_inc(wt_ps_ready, 1)

            transpose_w(0)
            x1_of(0, 0, 0, first=True)
            transpose_w(1)
            x1_of(1, 1, 0, first=True)
            pe.wait_ge(x1_ready, 1)
            for half in range(2):
                pe.wait_ge(a_ready, half + 1)
                for k in range(KC):
                    if k % 2 == 0:
                        pe.wait_ge(w_ready, 2 * half + k // 2 + 1)
                    last = main_chunk(0, k, halves=[half])
            last.then_inc(main_done, 1)
            x1_of(2, 0, 1)

            def step(u, s, n_x=None, first=False):
                wait_main(u, s, first)
                main_chunk(s, 0)
                main_chunk(s, 1, halves=[0])
                transpose_h(u - 1, 1 - s)
                main_chunk(s, 1, halves=[1])
                main_chunk(s, 2, halves=[0])
                lora(u - 1, 1 - s)
                main_chunk(s, 2, halves=[1])
                main_chunk(s, 3).then_inc(main_done, 1)
                if n_x is not None:
                    x1_of(u + 2, s, n_x)

            step(1, 1, 1, first=True)
            step(2, 0, 2)
            with pe.Fori(1, TILES // 2 - 2) as i:
                step(2 * i + 1, 1, i + 1)
                step(2 * i + 2, 0, i + 2)
            step(TILES - 3, 1, TILES // 2 - 1)
            step(TILES - 2, 0)

            def last_main_chunk(k, half):
                n = (HALF + 2 * AC, HALF)[half]
                return products(1, k, y_ps[1][:, half, 0:n], lambda lo_w: wa[:, k, lo_w, half, AC:AC + n])

            u = TILES - 1
            wait_main(u, 1)
            last_main_chunk(0, 0)
            last_main_chunk(1, 0)
            transpose_h(u - 1, 0)
            last_main_chunk(2, 0)
            last_main_chunk(3, 0).then_inc(main_done, 1)
            lora(u - 1, 0)
            last_main_chunk(0, 1)
            last_main_chunk(1, 1)
            transpose_h(u, 1)
            last_main_chunk(2, 1)
            last_main_chunk(3, 1)
            lora(u, 1, by_halves=True)


_INS = ["x", "itok_B_0_15", "itok_B_0_23", "L0_cond_weights", "L1_cond_W", "L1_cond_b",
        "L1_cond_lora_As", "L1_cond_lora_Bs"]


def kernel(**inputs):
    import numpy as _np
    import concourse.bacc as _bacc
    from concourse import mybir as _mybir
    from concourse.bass_utils import run_bass_kernel_spmd as _run

    nc = _bacc.Bacc("TRN2", target_bir_lowering=False, num_devices=1)
    arrays, args = {}, []
    for name in _INS:
        a = _np.ascontiguousarray(inputs[name])
        arrays[f"in_{name}"] = a
        args.append(nc.dram_tensor(f"in_{name}", a.shape, _mybir.dt.from_np(a.dtype), kind="ExternalInput").ap())
    shape = inputs["x"].shape
    args.append(nc.dram_tensor("out", shape, _mybir.dt.float32, kind="ExternalOutput").ap())
    lora_residual_program(nc, *args)
    r = _run(nc, [arrays], core_ids=[0])
    return r.results[0]["out"]
```
